# Optimizing a Trainium2 kernel written in Bass

```python
import numpy as np
import jax
import jax.numpy as jnp

def _softmax(x, axis=-1):
    return jax.nn.softmax(x, axis=axis)
def _gelu(x):
    return jax.nn.gelu(x, approximate=True)
def _silu(x):
    return jax.nn.silu(x)
def _sigmoid(x):
    return jax.nn.sigmoid(x)
def _layernorm(x, axis=-1, eps=1e-5):
    m = jnp.mean(x, axis=axis, keepdims=True)
    v = jnp.var(x, axis=axis, keepdims=True)
    return (x - m) / jnp.sqrt(v + eps)
def _scatter_add(tgt, idx, src, axis=0):
    return tgt.at[idx].add(src)
def _segment_sum(src, seg, n):
    return jax.ops.segment_sum(src, seg, n)

kernel_name = 'mk_adj_preln_d1_adj_128_309323'

def setup_inputs(seed: int = 0):
    np.random.seed(seed)
    _w = jnp.asarray
    def _rec_inputs():
        import jax
        import jax.numpy as jnp
        _gk = jax.random.key(seed)
        x = -0.000929 + 1 * jax.random.normal(jax.random.fold_in(_gk, 1), (8192, 128), jnp.float32)
        _w = (1.0 + jnp.arange(8192, dtype=jnp.float32)) ** -0.5
        _w = _w / _w.mean()
        _pij = jnp.clip(0.000976562 * _w[:, None] * _w[None, :], 0.0, 1.0)
        _a = jax.random.uniform(jax.random.fold_in(_gk, 2), (8192, 8192)) < _pij
        adj = _a.astype(jnp.int32)
        return x, adj
    x, adj = _rec_inputs()
    def _L0_gnn_setup():
        import jax, jax.numpy as jnp
        import numpy as np
        NEG_BIG = -9000000000000000.0
        LEAKY_SLOPE = 0.2
        key = jax.random.key(seed)
        k1, k2, k3 = jax.random.split(key, 3)
        N, M, D = (8192, 8192, 128)
        qs = jax.random.normal(k1, (N, D), dtype=jnp.float32)
        ks = jax.random.normal(k2, (M, D), dtype=jnp.float32)
        HpGraph_e_k = jax.random.randint(k3, (N, M), 0, 2, dtype=jnp.int32)
        return {'qs': qs, 'ks': ks, 'HpGraph_e_k': HpGraph_e_k}
    _L0_gnn_all = _L0_gnn_setup()
    _L0_gnn_in = {k: v for k, v in _L0_gnn_all.items() if k in ('ks', )}
    del _L0_gnn_all

    return {
        "x": x,
        "adj": adj,
        "L0_gnn_ks": _L0_gnn_in["ks"],
    }

def reference(x, adj, L0_gnn_ks):
    import jax
    import jax.numpy as jnp
    def _L0_gnn_ref(qs, ks, HpGraph_e_k):
        import jax, jax.numpy as jnp
        import numpy as np
        NEG_BIG = -9000000000000000.0
        LEAKY_SLOPE = 0.2
        scores = jnp.einsum('nd,md->nm', qs, ks)
        scores = jax.nn.leaky_relu(scores, negative_slope=LEAKY_SLOPE)
        scores = jnp.where(HpGraph_e_k > 0, scores, NEG_BIG)
        attn = jax.nn.softmax(scores, axis=1)
        return jnp.einsum('nm,md->nd', attn, ks)

    h = jnp.maximum(_layernorm(x, axis=-1), 0.0)
    x = x + _L0_gnn_ref(h, L0_gnn_ks, adj)
    return x


_drawn_inputs = setup_inputs


def setup_inputs(seed=0):
    import zlib

    import numpy as np

    out = dict(_drawn_inputs(seed))
    spreads = {}
    factors = {}
    for name, (base, spread) in spreads.items():
        noise = np.random.default_rng([zlib.crc32(name.encode()), seed]).standard_normal(out[name].shape)
        drawn = base * np.exp(spread * noise) if base else spread * noise
        out[name] = jnp.asarray(drawn.astype(out[name].dtype))
    for name, factor in factors.items():
        out[name] = (out[name] * factor).astype(out[name].dtype)
    return out
```

```python
import concourse.bass as bass
from concourse import mybir
from contextlib import ExitStack


def gat_kernel(nc: bass.Bass, x: bass.AP, adj: bass.AP, ks: bass.AP, out: bass.AP):
    fp32 = mybir.dt.float32
    fp16 = mybir.dt.float16
    bf16 = mybir.dt.bfloat16
    int32 = mybir.dt.int32
    ALU = mybir.AluOpType
    ACT = mybir.ActivationFunctionType
    AX = mybir.AxisListType

    N, D = x.shape
    M = ks.shape[0]
    P = 128
    TILES = N // P
    CHUNKS = M // P
    BLOCK = 512
    PER_BLOCK = BLOCK // P
    BLOCKS = M // BLOCK
    PAIR = 2 * BLOCK
    PAIRS = M // PAIR
    PER_PAIR = PAIR // P
    LOAD = 2 * PAIR
    LOADS = M // LOAD
    STAGES = 4
    STAGED = CHUNKS // STAGES
    SLOTS = 4
    T_SLOTS = 4
    T_LAG = 4
    OUT_LAG = 2

    EPS = 1e-5
    SLOPE = 0.2
    H_BITS, KEY_BITS, PROB_BITS = 10, 14, 14
    MASKED = -1e30
    LOWEST = -3e38
    EXPONENT = 0x7F800000
    TINY = 2.0 ** -60

    with ExitStack() as ctx:
        def sbuf(name, shape, dtype):
            return ctx.enter_context(nc.sbuf_tensor(name, shape, dtype))

        def psum(name, shape, dtype):
            return ctx.enter_context(nc.psum_tensor(name, shape, dtype))

        def sem(name):
            return ctx.enter_context(nc.semaphore(name))

        keys_in = sbuf("keys_in", [P, CHUNKS, D], fp32)
        keys = sbuf("keys", [P, CHUNKS, 2 * D], fp16)
        keysT_hi = sbuf("keysT_hi", [P, M], fp16)
        keysT_lo = sbuf("keysT_lo", [P, M], fp16)
        ident = sbuf("ident", [P, P], fp32)
        ones = sbuf("ones", [P, P], fp32)
        stage_max = sbuf("stage_max", [P, STAGES], fp32)
        part_max = sbuf("part_max", [P, 1], fp32)
        max_diag = sbuf("max_diag", [P, P], fp32)
        key_max = sbuf("key_max", [P, 1], fp32)
        key_pow2 = sbuf("key_pow2", [P, 1], fp32)
        inv_pow2 = sbuf("inv_pow2", [P, 1], fp32)
        key_scale = sbuf("key_scale", [P, 1], fp32)
        score_scale = sbuf("score_scale", [P, 1], fp32)
        out_scale = sbuf("out_scale", [P, 1], fp32)
        adj_in = sbuf("adj_in", [P, 2, LOAD], int32)
        mask = sbuf("mask", [P, 2, PAIR], bf16)
        scores = sbuf("scores", [P, 2, M], fp32)
        probs = sbuf("probs", [P, 2, PAIR], fp32)
        probsT_hi = sbuf("probsT_hi", [P, T_SLOTS, BLOCK], fp16)
        probsT_lo = sbuf("probsT_lo", [P, T_SLOTS, BLOCK], fp16)
        x_in = sbuf("x_in", [P, D], fp32)
        x_norm = sbuf("x_norm", [P, D], fp32)
        hT_hi = sbuf("hT_hi", [P, 2, P], fp16)
        hT_lo = sbuf("hT_lo", [P, 2, P], fp16)
        bn = sbuf("bn", [P, 6], fp32)
        mean_var = sbuf("mean_var", [P, 2], fp32)
        var_eps = sbuf("var_eps", [P, 1], fp32)
        rstd = sbuf("rstd", [P, 1], fp32)
        minus_half = sbuf("minus_half", [P, 1], fp32)
        block_max = sbuf("block_max", [P, BLOCKS], fp32)
        row_max = sbuf("row_max", [P, 1], fp32)
        neg_max = sbuf("neg_max", [P, 2], fp32)
        pair_sum = sbuf("pair_sum", [P, 2, PAIRS], fp32)
        row_sum = sbuf("row_sum", [P, 1], fp32)
        inv_sum = sbuf("inv_sum", [P, 1], fp32)
        weight = sbuf("weight", [P, 1], fp32)
        x_res = sbuf("x_res", [P, D], fp32)
        out_lo = sbuf("out_lo", [P, D], fp32)
        out_tile = sbuf("out_tile", [P, D], fp32)

        ps_scores = psum("ps_scores", [P, SLOTS, BLOCK], fp32)
        ps_T = psum("ps_T", [P, 2, BLOCK], fp32)
        ps_out = psum("ps_out", [P, 2, BLOCK], fp32)

        adj_loaded = [sem(f"adj_loaded{s}") for s in range(2)]
        keys_loaded = [sem(f"keys_loaded{s}") for s in range(STAGES)]
        x_loaded = sem("x_loaded")
        res_loaded = sem("res_loaded")
        stored = sem("stored")
        zeroed = sem("zeroed")
        consts_ready = sem("consts_ready")
        scale_steps = sem("scale_steps")
        max_spread = sem("max_spread")
        keysT_done = sem("keysT_done")
        keysT_hi_ready = sem("keysT_hi_ready")
        keysT_lo_ready = sem("keysT_lo_ready")
        keys_hi_ready = sem("keys_hi_ready")
        keys_lo_ready = sem("keys_lo_ready")
        bn_done = sem("bn_done")
        stats_ready = sem("stats_ready")
        eps_added = sem("eps_added")
        rstd_ready = sem("rstd_ready")
        norm_ready = sem("norm_ready")
        hT_done = sem("hT_done")
        hT_hi_ready = sem("hT_hi_ready")
        hT_ready = sem("hT_ready")
        mask_ready = sem("mask_ready")
        scores_done = sem("scores_done")
        relu_ready = sem("relu_ready")
        masked_ready = sem("masked_ready")
        leaky_ready = sem("leaky_ready")
        max_ready = sem("max_ready")
        neg_max_ready = sem("neg_max_ready")
        probs_ready = sem("probs_ready")
        sum_ready = sem("sum_ready")
        inv_ready = sem("inv_ready")
        weight_ready = sem("weight_ready")
        T_done = sem("T_done")
        T_hi_ready = sem("T_hi_ready")
        T_lo_ready = sem("T_lo_ready")
        out_done = sem("out_done")
        lo_scaled = sem("lo_scaled")
        out_ready = sem("out_ready")

        CONSTS = 3
        SCALED = STAGES + 9

        def rows(t):
            return bass.ds(t * P, P)

        def is_tile(t, n):
            return isinstance(t, int) and t == n

        def cols(b):
            return slice(b * BLOCK, (b + 1) * BLOCK)

        block = ctx.enter_context(nc.Block())

        def steps(engine, step):
            step(-1, 1, more=True, this=False, prev=False, ahead=True)
            step(0, 0, more=True, this=True, prev=False, ahead=True)
            with engine.Fori(1, TILES - 3, 2) as i:
                step(i, 1, more=True, this=True, prev=True, ahead=True)
                step(i + 1, 0, more=True, this=True, prev=True, ahead=True)
            step(TILES - 3, 1, more=True, this=True, prev=True, ahead=True)
            step(TILES - 2, 0, more=True, this=True, prev=True, ahead=False)
            step(TILES - 1, 1, more=False, this=True, prev=True, ahead=False)
            step(TILES, 0, more=False, this=False, prev=True, ahead=False)

        def behind(i, odd, j, lag, this, prev):
            if j >= lag:
                return (i, odd, j - lag) if this else None
            return (i - 1, 1 - odd, j - lag + BLOCKS) if prev else None

        @block.sync
        def _(sp):
            key_chunks = ks.rearrange("(c p) d -> p c d", p=P)

            def load_x(t):
                if not is_tile(t, 0):
                    sp.wait_ge(norm_ready, t)
                sp.dma_start(x_in[:, :], x[rows(t), :]).then_inc(x_loaded, 16)

            def load_residual(t):
                if not is_tile(t, 0):
                    sp.wait_ge(out_ready, t)
                sp.dma_start(x_res[:, :], x[rows(t), :]).then_inc(res_loaded, 16)

            def store(t):
                sp.wait_ge(out_ready, t + 1)
                sp.dma_start(out[rows(t), :], out_tile[:, :]).then_inc(stored, 16)

            def load_adj(q, k):
                if not is_tile(q, 0) or k >= 2:
                    sp.wait_ge(mask_ready, q * PAIRS + 2 * k - 2)
                sp.dma_start(adj_in[:, k % 2, :], adj[rows(q), k * LOAD:(k + 1) * LOAD]) \
                    .then_inc(adj_loaded[k % 2], 16)

            load_x(0)
            for s in range(STAGES):
                for half in range(2):
                    c = slice((2 * s + half) * STAGED // 2, (2 * s + half + 1) * STAGED // 2)
                    sp.dma_start(keys_in[:, c, :], key_chunks[:, c, :]).then_inc(keys_loaded[s], 16)
            load_residual(0)

            def step(i, odd, more, this, prev, ahead):
                for k in range(LOADS):
                    if more:
                        load_adj(i + 1, k)
                    if k == 1 and ahead:
                        load_x(i + 2)
                    if k == 3 and prev:
                        store(i - 1)
                        if not is_tile(i, TILES):
                            load_residual(i)

            steps(sp, step)
            sp.wait_ge(stored, 16 * TILES)

        @block.gpsimd
        def _(pool):
            nc.gpsimd.memset(ident[:, :], 0.0).then_inc(zeroed, 1)
            nc.gpsimd.memset(ones[:, :], 1.0).then_inc(consts_ready, 1)
            nc.gpsimd.memset(minus_half[:, :], -0.5).then_inc(consts_ready, 1)
            pool.wait_ge(zeroed, 1)
            nc.gpsimd.affine_select(out=ident[:, :], in_=ident[:, :], compare_op=ALU.not_equal, fill=1.0,
                                    base=0, pattern=[[-1, P]], channel_multiplier=1).then_inc(consts_ready, 1)
            pool.wait_ge(consts_ready, CONSTS)

            def reciprocal_std(t):
                pool.wait_ge(stats_ready, t + 1)
                if not is_tile(t, 0):
                    pool.wait_ge(norm_ready, t)
                pool.nop(nofuse=True)
                nc.gpsimd.tensor_scalar(var_eps[:, :], mean_var[:, 1:2], EPS, 2.0 ** (-2 * H_BITS),
                                        ALU.add, ALU.mult).then_inc(eps_added, 1)
                pool.wait_ge(eps_added, t + 1)
                nc.gpsimd.tensor_tensor(rstd[:, :], var_eps[:, :], minus_half[:, :], ALU.pow) \
                    .then_inc(rstd_ready, 1)

            def add_mask(q, odd, b):
                pool.wait_ge(relu_ready, q * BLOCKS + b + 1)
                pool.wait_ge(mask_ready, q * PAIRS + b // 2 + 1)
                s = scores[:, odd, cols(b)]
                nc.gpsimd.tensor_tensor(s, s, mask[:, (b // 2) % 2, (b % 2) * BLOCK:(b % 2 + 1) * BLOCK], ALU.add) \
                    .then_inc(masked_ready, 1)

            reciprocal_std(0)

            def step(i, odd, more, this, prev, ahead):
                for j in range(BLOCKS):
                    if more:
                        add_mask(i + 1, 1 - odd, j)
                    if j == 6 and ahead:
                        reciprocal_std(i + 2)

            steps(pool, step)

        @block.tensor
        def _(pe):
            pe.wait_ge(consts_ready, CONSTS)

            def transpose_h(t, odd):
                pe.wait_ge(norm_ready, t + 1)
                if not (is_tile(t, 0) or is_tile(t, 1)):
                    pe.wait_ge(out_ready, t - 2)
                nc.tensor.transpose(ps_out[:, 1 - odd, 0:P], x_norm[:, :], ident[:, :]).then_inc(hT_done, 1)

            def transpose_keys(b):
                if b >= 2:
                    pe.wait_ge(keysT_lo_ready, b - 1)
                for k in range(PER_BLOCK):
                    mm = nc.tensor.transpose(ps_T[:, b % 2, k * P:(k + 1) * P],
                                             keys_in[:, b * PER_BLOCK + k, :], ident[:, :])
                mm.then_inc(keysT_done, 1)

            def score_block(q, odd, b):
                if b == 0:
                    pe.wait_ge(hT_ready, q + 1)
                if is_tile(q, 0):
                    pe.wait_ge(keysT_hi_ready, b + 1)
                    pe.wait_ge(keysT_lo_ready, b + 1)
                if not is_tile(q, 0) or b >= SLOTS:
                    pe.wait_ge(leaky_ready, q * BLOCKS + b - SLOTS + 1)
                dst = ps_scores[:, b % SLOTS, :]
                nc.tensor.matmul(dst, hT_hi[:, odd, :], keysT_hi[:, cols(b)], start=True, stop=False)
                nc.tensor.matmul(dst, hT_hi[:, odd, :], keysT_lo[:, cols(b)], start=False, stop=False)
                nc.tensor.matmul(dst, hT_lo[:, odd, :], keysT_hi[:, cols(b)], start=False, stop=True) \
                    .then_inc(scores_done, 1)

            def transpose_probs(t, b):
                if b % 2 == 0:
                    pe.wait_ge(probs_ready, t * PAIRS + b // 2 + 1)
                if not is_tile(t, 0) or b >= 2:
                    pe.wait_ge(T_lo_ready, t * BLOCKS + b - 1)
                for k in range(PER_BLOCK):
                    at = (b % 2) * BLOCK + k * P
                    mm = nc.tensor.transpose(ps_T[:, b % 2, k * P:(k + 1) * P],
                                             probs[:, (b // 2) % 2, at:at + P], ident[:, :])
                mm.then_inc(T_done, 1)

            def output_block(t, odd, b):
                pe.wait_ge(T_hi_ready, t * BLOCKS + b + 1)
                pe.wait_ge(T_lo_ready, t * BLOCKS + b + 1)
                if is_tile(t, 0) and b % 2 == 0:
                    pe.wait_ge(keys_lo_ready, b // 2 + 1)
                if b == 0 and not (is_tile(t, 0) or is_tile(t, 1)):
                    pe.wait_ge(out_ready, t - 1)
                o = ps_out[:, odd, :]
                for k in range(PER_BLOCK):
                    c = b * PER_BLOCK + k
                    hi_part = probsT_hi[:, b % T_SLOTS, k * P:(k + 1) * P]
                    lo_part = probsT_lo[:, b % T_SLOTS, k * P:(k + 1) * P]
                    if c < CHUNKS - 1:
                        nc.tensor.matmul(o[:, 0:2 * D], hi_part, keys[:, c, :], start=(c == 0), stop=False)
                        mm = nc.tensor.matmul(o[:, 0:D], lo_part, keys[:, c, 0:D], start=False, stop=False)
                    else:
                        nc.tensor.matmul(o[:, 0:D], lo_part, keys[:, c, 0:D], start=False, stop=False)
                        mm = nc.tensor.matmul(o[:, 0:2 * D], hi_part, keys[:, c, :], start=False, stop=True)
                mm.then_inc(out_done, 1)

            transpose_h(0, 0)
            pe.wait_ge(scale_steps, STAGES + 2)
            pe.wait_ge(hT_ready, 1)
            nc.tensor.matmul(ps_out[:, 0, 0:P], ones[:, :], max_diag[:, :], start=True, stop=True) \
                .then_inc(max_spread, 1)
            transpose_keys(0)
            transpose_keys(1)

            def step(i, odd, more, this, prev, ahead):
                for j in range(BLOCKS):
                    if more:
                        if is_tile(i, -1) and j + 2 < BLOCKS:
                            transpose_keys(j + 2)
                        score_block(i + 1, 1 - odd, j)
                    turned = behind(i, odd, j, T_LAG, this, prev)
                    if turned:
                        transpose_probs(turned[0], turned[2])
                    added = behind(i, odd, j, T_LAG + OUT_LAG, this, prev)
                    if added:
                        output_block(*added)
                    if j == 11 and ahead:
                        transpose_h(i + 2, odd)

            steps(pe, step)

        @block.scalar
        def _(act):
            act.wait_ge(scale_steps, SCALED)

            def split_keysT_hi(b):
                act.wait_ge(keysT_done, b + 1)
                nc.scalar.activation(keysT_hi[:, cols(b)], ps_T[:, b % 2, :], ACT.Copy, scale=key_scale[:, :]) \
                    .then_inc(keysT_hi_ready, 1)

            def split_keys_hi(p):
                c = slice(p * PER_PAIR, (p + 1) * PER_PAIR)
                nc.scalar.activation(keys[:, c, 0:D], keys_in[:, c, :], ACT.Copy, scale=key_scale[:, :]) \
                    .then_inc(keys_hi_ready, 1)

            def relu(q, odd, b):
                act.wait_ge(scores_done, q * BLOCKS + b + 1)
                if not (is_tile(q, 0) or is_tile(q, 1)):
                    act.wait_ge(probs_ready, (q - 2) * PAIRS + b // 2 + 1)
                nc.scalar.activation(scores[:, odd, cols(b)], ps_scores[:, b % SLOTS, :], ACT.Relu,
                                     scale=1.0 / SLOPE - 1.0).then_inc(relu_ready, 1)

            def exponentials(t, odd, p):
                if p == 0:
                    act.wait_ge(neg_max_ready, t + 1)
                    if not (is_tile(t, 0) or is_tile(t, 1)):
                        act.wait_ge(sum_ready, t - 1)
                if not is_tile(t, 0) or p >= 2:
                    act.wait_ge(T_done, t * BLOCKS + 2 * p - 2)
                nc.scalar.activation(probs[:, p % 2, :], scores[:, odd, p * PAIR:(p + 1) * PAIR], ACT.Exp,
                                     bias=neg_max[:, odd:odd + 1], scale=1.0,
                                     accum_out=pair_sum[:, odd, p:p + 1]) \
                    .then_inc(probs_ready, 1)

            def split_probs_hi(t, b):
                act.wait_ge(T_done, t * BLOCKS + b + 1)
                if not is_tile(t, 0) or b >= T_SLOTS:
                    act.wait_ge(out_done, t * BLOCKS + b - T_SLOTS + 1)
                nc.scalar.activation(probsT_hi[:, b % T_SLOTS, :], ps_T[:, b % 2, :], ACT.Copy,
                                     scale=2.0 ** PROB_BITS).then_inc(T_hi_ready, 1)

            split_keysT_hi(0)
            split_keysT_hi(1)

            def step(i, odd, more, this, prev, ahead):
                for j in range(BLOCKS):
                    if is_tile(i, -1):
                        if j + 2 < BLOCKS:
                            split_keysT_hi(j + 2)
                        if j % 2 == 1:
                            split_keys_hi(j // 2)
                    if more:
                        relu(i + 1, 1 - odd, j)
                    turned = behind(i, odd, j, T_LAG, this, prev)
                    if turned:
                        split_probs_hi(turned[0], turned[2])
                    if j % 2 == 0:
                        made = behind(i, odd, j, T_LAG - 2, this, prev)
                        if made:
                            exponentials(made[0], made[1], made[2] // 2)

            steps(act, step)

        @block.vector
        def _(dve):
            def statistics(t):
                dve.wait_ge(x_loaded, 16 * t + 16)
                nc.vector.bn_stats(bn[:, :], x_in[:, :]).then_inc(bn_done, 1)
                dve.wait_ge(bn_done, t + 1)
                if not is_tile(t, 0):
                    dve.wait_ge(rstd_ready, t)
                dve.nop(nofuse=True)
                nc.vector.bn_aggr(mean_var[:, :], bn[:, :]).then_inc(stats_ready, 1)

            def normalise(t):
                dve.wait_ge(rstd_ready, t + 1)
                if not is_tile(t, 0):
                    dve.wait_ge(hT_done, t)
                nc.vector.tensor_scalar(x_norm[:, :], x_in[:, :], mean_var[:, 0:1], rstd[:, 0:1],
                                        ALU.subtract, ALU.mult).then_inc(norm_ready, 1)

            def split_h(t, odd):
                dve.wait_ge(hT_done, t + 1)
                if not (is_tile(t, 0) or is_tile(t, 1)):
                    dve.wait_ge(scores_done, (t - 1) * BLOCKS)
                src = ps_out[:, 1 - odd, 0:P]
                nc.vector.tensor_scalar(hT_hi[:, odd, :], src, 0.0, None, ALU.max).then_inc(hT_hi_ready, 1)
                dve.wait_ge(hT_hi_ready, t + 1)
                nc.vector.scalar_tensor_tensor(out=hT_lo[:, odd, :], in0=src, scalar=0.0, in1=hT_hi[:, odd, :],
                                               op0=ALU.max, op1=ALU.subtract).then_inc(hT_ready, 1)

            def find_scales():
                for s in range(STAGES):
                    dve.wait_ge(keys_loaded[s], 32)
                    nc.vector.tensor_reduce(stage_max[:, s:s + 1], keys_in[:, s * STAGED:(s + 1) * STAGED, :],
                                            axis=AX.XY, op=ALU.max, apply_absolute_value=True) \
                        .then_inc(scale_steps, 1)
                dve.wait_ge(scale_steps, STAGES)
                nc.vector.tensor_reduce(part_max[:, :], stage_max[:, :], axis=AX.X, op=ALU.max) \
                    .then_inc(scale_steps, 1)
                dve.wait_ge(scale_steps, STAGES + 1)
                nc.vector.tensor_scalar(max_diag[:, :], ident[:, :], part_max[:, 0:1], None, ALU.mult) \
                    .then_inc(scale_steps, 1)
                dve.wait_ge(max_spread, 1)
                nc.vector.tensor_reduce(key_max[:, :], ps_out[:, 0, 0:P], axis=AX.X, op=ALU.max) \
                    .then_inc(scale_steps, 1)
                dve.wait_ge(scale_steps, STAGES + 3)
                nc.vector.tensor_scalar(key_pow2[:, :].bitcast(int32), key_max[:, :].bitcast(int32), EXPONENT, None,
                                        ALU.bitwise_and).then_inc(scale_steps, 1)
                dve.wait_ge(scale_steps, STAGES + 4)
                nc.vector.tensor_scalar(key_pow2[:, :], key_pow2[:, :], TINY, None, ALU.max) \
                    .then_inc(scale_steps, 1)
                dve.wait_ge(scale_steps, STAGES + 5)
                nc.vector.reciprocal(inv_pow2[:, :], key_pow2[:, :]).then_inc(scale_steps, 1)
                nc.vector.tensor_scalar(score_scale[:, :], key_pow2[:, :], SLOPE * 2.0 ** (-H_BITS - KEY_BITS), None,
                                        ALU.mult).then_inc(scale_steps, 1)
                nc.vector.tensor_scalar(out_scale[:, :], key_pow2[:, :], 2.0 ** (-PROB_BITS - KEY_BITS), None,
                                        ALU.mult).then_inc(scale_steps, 1)
                dve.wait_ge(scale_steps, STAGES + 6)
                nc.vector.tensor_scalar(key_scale[:, :], inv_pow2[:, :], 2.0 ** KEY_BITS, None, ALU.mult) \
                    .then_inc(scale_steps, 1)
                dve.wait_ge(scale_steps, SCALED)

            def split_keysT_lo(b):
                dve.wait_ge(keysT_hi_ready, b + 1)
                nc.vector.scalar_tensor_tensor(out=keysT_lo[:, cols(b)], in0=ps_T[:, b % 2, :], scalar=key_scale[:, 0:1],
                                               in1=keysT_hi[:, cols(b)], op0=ALU.mult, op1=ALU.subtract) \
                    .then_inc(keysT_lo_ready, 1)

            def split_keys_lo(p):
                c = slice(p * PER_PAIR, (p + 1) * PER_PAIR)
                dve.wait_ge(keys_hi_ready, p + 1)
                nc.vector.scalar_tensor_tensor(out=keys[:, c, D:2 * D], in0=keys_in[:, c, :], scalar=key_scale[:, 0:1],
                                               in1=keys[:, c, 0:D], op0=ALU.mult, op1=ALU.subtract) \
                    .then_inc(keys_lo_ready, 1)

            def make_mask(q, p):
                k = p // 2
                dve.wait_ge(adj_loaded[k % 2], (q * (LOADS // 2) + k // 2 + 1) * 16)
                if not is_tile(q, 0) or p >= 2:
                    dve.wait_ge(masked_ready, q * BLOCKS + 2 * p - 2)
                nc.vector.tensor_scalar(mask[:, p % 2, :], adj_in[:, k % 2, (p % 2) * PAIR:(p % 2 + 1) * PAIR],
                                        0.0, MASKED, ALU.is_le, ALU.mult).then_inc(mask_ready, 1)

            def leaky(q, odd, b):
                dve.wait_ge(masked_ready, q * BLOCKS + b + 1)
                if b == 0 and not is_tile(q, 0):
                    dve.wait_ge(max_ready, q)
                dve.nop(nofuse=True)
                s = scores[:, odd, cols(b)]
                nc.vector.tensor_tensor_reduce(out=s, in0=ps_scores[:, b % SLOTS, :], in1=s, scale=score_scale[:, 0:1],
                                               scalar=LOWEST, op0=ALU.add, op1=ALU.max,
                                               accum_out=block_max[:, b:b + 1]).then_inc(leaky_ready, 1)

            def split_probs_lo(t, b):
                dve.wait_ge(T_hi_ready, t * BLOCKS + b + 1)
                nc.vector.scalar_tensor_tensor(out=probsT_lo[:, b % T_SLOTS, :], in0=ps_T[:, b % 2, :],
                                               scalar=2.0 ** PROB_BITS, in1=probsT_hi[:, b % T_SLOTS, :],
                                               op0=ALU.mult, op1=ALU.subtract).then_inc(T_lo_ready, 1)

            def maximum(q, odd):
                dve.wait_ge(leaky_ready, (q + 1) * BLOCKS)
                nc.vector.tensor_reduce(row_max[:, :], block_max[:, :], axis=AX.X, op=ALU.max).then_inc(max_ready, 1)
                dve.wait_ge(max_ready, q + 1)
                if not (is_tile(q, 0) or is_tile(q, 1)):
                    dve.wait_ge(probs_ready, (q - 1) * PAIRS)
                nc.vector.tensor_scalar(neg_max[:, odd:odd + 1], row_max[:, :], -1.0, None, ALU.mult) \
                    .then_inc(neg_max_ready, 1)

            def weigh(t, odd):
                dve.wait_ge(probs_ready, (t + 1) * PAIRS)
                nc.vector.tensor_reduce(row_sum[:, :], pair_sum[:, odd, :], axis=AX.X, op=ALU.add).then_inc(sum_ready, 1)
                dve.wait_ge(sum_ready, t + 1)
                nc.vector.reciprocal(inv_sum[:, :], row_sum[:, :]).then_inc(inv_ready, 1)
                dve.wait_ge(inv_ready, t + 1)
                nc.vector.tensor_scalar(weight[:, :], inv_sum[:, :], out_scale[:, 0:1], None, ALU.mult) \
                    .then_inc(weight_ready, 1)

            def finish(t, odd):
                dve.wait_ge(out_done, (t + 1) * BLOCKS)
                dve.wait_ge(res_loaded, 16 * t + 16)
                dve.wait_ge(weight_ready, t + 1)
                nc.vector.scalar_tensor_tensor(out=out_lo[:, :], in0=ps_out[:, odd, D:2 * D], scalar=weight[:, 0:1],
                                               in1=x_res[:, :], op0=ALU.mult, op1=ALU.add).then_inc(lo_scaled, 1)
                dve.wait_ge(lo_scaled, t + 1)
                if not is_tile(t, 0):
                    dve.wait_ge(stored, 16 * t)
                nc.vector.scalar_tensor_tensor(out=out_tile[:, :], in0=ps_out[:, odd, 0:D], scalar=weight[:, 0:1],
                                               in1=out_lo[:, :], op0=ALU.mult, op1=ALU.add).then_inc(out_ready, 1)

            dve.wait_ge(consts_ready, CONSTS)
            statistics(0)
            normalise(0)
            split_h(0, 0)
            find_scales()
            make_mask(0, 0)
            split_keysT_lo(0)
            split_keysT_lo(1)

            def step(i, odd, more, this, prev, ahead):
                for j in range(BLOCKS):
                    p = j // 2
                    if is_tile(i, -1) and j + 2 < BLOCKS:
                        split_keysT_lo(j + 2)
                    if is_tile(i, 0) and j % 2 == 0:
                        split_keys_lo(p)
                    turned = behind(i, odd, j, T_LAG, this, prev)
                    if turned:
                        split_probs_lo(turned[0], turned[2])
                    if more and j % 2 == 0:
                        if p + 1 < PAIRS:
                            make_mask(i + 1, p + 1)
                        elif not is_tile(i, TILES - 2):
                            make_mask(i + 2, 0)
                    if ahead:
                        if j == 3:
                            statistics(i + 2)
                        if j == 9:
                            normalise(i + 2)
                        if j == 13:
                            split_h(i + 2, odd)
                    if prev and j == 3:
                        weigh(i - 1, 1 - odd)
                    if prev and j == 6:
                        finish(i - 1, 1 - odd)
                    if more:
                        leaky(i + 1, 1 - odd, j)
                if more:
                    maximum(i + 1, 1 - odd)

            steps(dve, step)


_INS = ["x", "adj", "L0_gnn_ks"]


def kernel(**inputs):
    import numpy as _np
    import concourse.bacc as _bacc
    from concourse import mybir as _mybir
    from concourse.bass_utils import run_bass_kernel_spmd as _run

    nc = _bacc.Bacc("TRN2", target_bir_lowering=False, num_devices=1)
    arrays, args = {}, []
    for name in _INS:
        a = _np.ascontiguousarray(inputs[name])
        arrays[f"in_{name}_dram"] = a
        args.append(nc.dram_tensor(f"in_{name}_dram", a.shape, _mybir.dt.from_np(a.dtype), kind="ExternalInput").ap())
    shape = inputs["x"].shape
    args.append(nc.dram_tensor("out_dram", shape, _mybir.dt.float32, kind="ExternalOutput").ap())
    gat_kernel(nc, *args)
    r = _run(nc, [arrays], core_ids=[0])
    return r.results[0]["out_dram"]
```

```python
import concourse.bass as bass
from concourse import mybir
from contextlib import ExitStack


def gat_kernel(nc: bass.Bass, x: bass.AP, adj: bass.AP, ks: bass.AP, out: bass.AP):
    fp32 = mybir.dt.float32
    fp16 = mybir.dt.float16
    bf16 = mybir.dt.bfloat16
    int32 = mybir.dt.int32
    ALU = mybir.AluOpType
    ACT = mybir.ActivationFunctionType
    AX = mybir.AxisListType

    N, D = x.shape
    M = ks.shape[0]
    P = 128
    TILES = N // P
    CHUNKS = M // P
    BLOCK = 512
    PER_BLOCK = BLOCK // P
    BLOCKS = M // BLOCK
    PAIR = 2 * BLOCK
    PAIRS = M // PAIR
    PER_PAIR = PAIR // P
    LOAD = 2 * PAIR
    LOADS = M // LOAD
    SLOTS = 4
    T_SLOTS = 4
    T_LAG = 4
    OUT_LAG = 2

    EPS = 1e-5
    SLOPE = 0.2
    H_BITS, KEY_BITS, PROB_BITS = 10, 14, 14
    MASKED = -1e30
    LOWEST = -3e38
    EXPONENT = 0x7F800000
    TINY = 2.0 ** -60

    with ExitStack() as ctx:
        def sbuf(name, shape, dtype):
            return ctx.enter_context(nc.sbuf_tensor(name, shape, dtype))

        def psum(name, shape, dtype):
            return ctx.enter_context(nc.psum_tensor(name, shape, dtype))

        def sem(name):
            return ctx.enter_context(nc.semaphore(name))

        keys_in = sbuf("keys_in", [P, CHUNKS, D], fp32)
        keys = sbuf("keys", [P, CHUNKS, 2 * D], fp16)
        keysT_hi = sbuf("keysT_hi", [P, M], fp16)
        keysT_lo = sbuf("keysT_lo", [P, M], fp16)
        ident = sbuf("ident", [P, P], fp32)
        ones = sbuf("ones", [P, P], fp32)
        load_max = sbuf("load_max", [P, PAIRS], fp32)
        part_max = sbuf("part_max", [P, 1], fp32)
        max_diag = sbuf("max_diag", [P, P], fp32)
        key_max = sbuf("key_max", [P, 1], fp32)
        key_pow2 = sbuf("key_pow2", [P, 1], fp32)
        inv_pow2 = sbuf("inv_pow2", [P, 1], fp32)
        key_scale = sbuf("key_scale", [P, 1], fp32)
        score_scale = sbuf("score_scale", [P, 1], fp32)
        out_scale = sbuf("out_scale", [P, 1], fp32)
        adj_in = sbuf("adj_in", [P, 2, LOAD], int32)
        mask = sbuf("mask", [P, 2, PAIR], bf16)
        scores = sbuf("scores", [P, 2, M], fp32)
        probs = sbuf("probs", [P, 2, PAIR], fp32)
        probsT_hi = sbuf("probsT_hi", [P, T_SLOTS, BLOCK], fp16)
        probsT_lo = sbuf("probsT_lo", [P, T_SLOTS, BLOCK], fp16)
        x_in = sbuf("x_in", [P, D], fp32)
        x_norm = sbuf("x_norm", [P, D], fp32)
        hT_hi = sbuf("hT_hi", [P, 2, P], fp16)
        hT_lo = sbuf("hT_lo", [P, 2, P], fp16)
        bn = sbuf("bn", [P, 6], fp32)
        mean_var = sbuf("mean_var", [P, 2], fp32)
        var_eps = sbuf("var_eps", [P, 1], fp32)
        rstd = sbuf("rstd", [P, 1], fp32)
        minus_half = sbuf("minus_half", [P, 1], fp32)
        pair_max = sbuf("pair_max", [P, PAIRS], fp32)
        row_max = sbuf("row_max", [P, 1], fp32)
        neg_max = sbuf("neg_max", [P, 2], fp32)
        pair_sum = sbuf("pair_sum", [P, 2, PAIRS], fp32)
        row_sum = sbuf("row_sum", [P, 1], fp32)
        inv_sum = sbuf("inv_sum", [P, 1], fp32)
        weight = sbuf("weight", [P, 1], fp32)
        x_res = sbuf("x_res", [P, D], fp32)
        out_lo = sbuf("out_lo", [P, D], fp32)
        out_tile = sbuf("out_tile", [P, D], fp32)

        ps_scores = psum("ps_scores", [P, SLOTS, BLOCK], fp32)
        ps_T = psum("ps_T", [P, 2, BLOCK], fp32)
        ps_out = psum("ps_out", [P, 2, BLOCK], fp32)

        adj_loaded = [sem(f"adj_loaded{s}") for s in range(2)]
        keys_loaded = [sem(f"keys_loaded{p}") for p in range(PAIRS)]
        x_loaded = sem("x_loaded")
        res_loaded = sem("res_loaded")
        stored = sem("stored")
        zeroed = sem("zeroed")
        consts_ready = sem("consts_ready")
        scale_steps = sem("scale_steps")
        max_spread = sem("max_spread")
        keysT_done = sem("keysT_done")
        keysT_copied = sem("keysT_copied")
        keysT_hi_ready = sem("keysT_hi_ready")
        keysT_lo_ready = sem("keysT_lo_ready")
        keys_hi_ready = sem("keys_hi_ready")
        keys_lo_ready = sem("keys_lo_ready")
        bn_done = sem("bn_done")
        stats_ready = sem("stats_ready")
        eps_added = sem("eps_added")
        rstd_ready = sem("rstd_ready")
        norm_ready = sem("norm_ready")
        hT_done = sem("hT_done")
        hT_hi_ready = sem("hT_hi_ready")
        hT_ready = sem("hT_ready")
        mask_ready = sem("mask_ready")
        scores_done = sem("scores_done")
        relu_ready = sem("relu_ready")
        masked_ready = sem("masked_ready")
        leaky_ready = sem("leaky_ready")
        max_ready = sem("max_ready")
        neg_max_ready = sem("neg_max_ready")
        probs_ready = sem("probs_ready")
        sum_ready = sem("sum_ready")
        inv_ready = sem("inv_ready")
        weight_ready = sem("weight_ready")
        T_done = sem("T_done")
        T_hi_ready = sem("T_hi_ready")
        T_lo_ready = sem("T_lo_ready")
        out_done = sem("out_done")
        lo_scaled = sem("lo_scaled")
        out_ready = sem("out_ready")

        CONSTS = 3
        SCALED = PAIRS + 9

        def rows(t):
            return bass.ds(t * P, P)

        def is_tile(t, n):
            return isinstance(t, int) and t == n

        def cols(b):
            return slice(b * BLOCK, (b + 1) * BLOCK)

        def pair_cols(p):
            return slice(p * PAIR, (p + 1) * PAIR)

        keysT = scores[:, 1, :]

        block = ctx.enter_context(nc.Block())

        def steps(engine, step):
            step(-1, 1, more=True, this=False, prev=False, ahead=True)
            step(0, 0, more=True, this=True, prev=False, ahead=True)
            step(1, 1, more=True, this=True, prev=True, ahead=True)
            with engine.Fori(2, TILES - 3, 2) as i:
                step(i, 0, more=True, this=True, prev=True, ahead=True)
                step(i + 1, 1, more=True, this=True, prev=True, ahead=True)
            step(TILES - 2, 0, more=True, this=True, prev=True, ahead=False)
            step(TILES - 1, 1, more=False, this=True, prev=True, ahead=False)
            step(TILES, 0, more=False, this=False, prev=True, ahead=False)

        def behind(i, odd, j, lag, this, prev):
            if j >= lag:
                return (i, odd, j - lag) if this else None
            return (i - 1, 1 - odd, j - lag + BLOCKS) if prev else None

        @block.sync
        def _(sp):
            key_chunks = ks.rearrange("(c p) d -> p c d", p=P)

            def load_x(t):
                if not is_tile(t, 0):
                    sp.wait_ge(norm_ready, t)
                sp.dma_start(x_in[:, :], x[rows(t), :]).then_inc(x_loaded, 16)

            def load_residual(t):
                if not is_tile(t, 0):
                    sp.wait_ge(out_ready, t)
                sp.dma_start(x_res[:, :], x[rows(t), :]).then_inc(res_loaded, 16)

            def store(t):
                sp.wait_ge(out_ready, t + 1)
                sp.dma_start(out[rows(t), :], out_tile[:, :]).then_inc(stored, 16)

            def load_adj(q, k):
                if not is_tile(q, 0) or k >= 2:
                    sp.wait_ge(mask_ready, q * PAIRS + 2 * k - 2)
                sp.dma_start(adj_in[:, k % 2, :], adj[rows(q), k * LOAD:(k + 1) * LOAD]) \
                    .then_inc(adj_loaded[k % 2], 16)

            load_x(0)
            for p in range(PAIRS):
                c = slice(p * PER_PAIR, (p + 1) * PER_PAIR)
                sp.dma_start(keys_in[:, c, :], key_chunks[:, c, :]).then_inc(keys_loaded[p], 16)
            load_residual(0)

            def step(i, odd, more, this, prev, ahead):
                for k in range(LOADS):
                    if more:
                        load_adj(i + 1, k)
                    if k == 1 and ahead:
                        load_x(i + 2)
                    if k == 3 and prev:
                        store(i - 1)
                        if not is_tile(i, TILES):
                            load_residual(i)

            steps(sp, step)
            sp.wait_ge(stored, 16 * TILES)

        @block.gpsimd
        def _(pool):
            nc.gpsimd.memset(ident[:, :], 0.0).then_inc(zeroed, 1)
            nc.gpsimd.memset(ones[:, :], 1.0).then_inc(consts_ready, 1)
            nc.gpsimd.memset(minus_half[:, :], -0.5).then_inc(consts_ready, 1)
            pool.wait_ge(zeroed, 1)
            nc.gpsimd.affine_select(out=ident[:, :], in_=ident[:, :], compare_op=ALU.not_equal, fill=1.0,
                                    base=0, pattern=[[-1, P]], channel_multiplier=1).then_inc(consts_ready, 1)
            pool.wait_ge(consts_ready, CONSTS)

            def reciprocal_std(t):
                pool.wait_ge(stats_ready, t + 1)
                if not is_tile(t, 0):
                    pool.wait_ge(norm_ready, t)
                pool.nop(nofuse=True)
                nc.gpsimd.tensor_scalar(var_eps[:, :], mean_var[:, 1:2], EPS, 2.0 ** (-2 * H_BITS),
                                        ALU.add, ALU.mult).then_inc(eps_added, 1)
                pool.wait_ge(eps_added, t + 1)
                nc.gpsimd.tensor_tensor(rstd[:, :], var_eps[:, :], minus_half[:, :], ALU.pow) \
                    .then_inc(rstd_ready, 1)

            def add_mask(q, odd, b):
                pool.wait_ge(relu_ready, q * BLOCKS + b + 1)
                pool.wait_ge(mask_ready, q * PAIRS + b // 2 + 1)
                s = scores[:, odd, cols(b)]
                nc.gpsimd.tensor_tensor(s, s, mask[:, (b // 2) % 2, (b % 2) * BLOCK:(b % 2 + 1) * BLOCK], ALU.add) \
                    .then_inc(masked_ready, 1)

            reciprocal_std(0)

            def step(i, odd, more, this, prev, ahead):
                for j in range(BLOCKS):
                    if more:
                        add_mask(i + 1, 1 - odd, j)
                    if j == 7 and ahead:
                        reciprocal_std(i + 2)

            steps(pool, step)

        @block.tensor
        def _(pe):
            pe.wait_ge(consts_ready, CONSTS)

            def transpose_h(t, odd):
                pe.wait_ge(norm_ready, t + 1)
                if not (is_tile(t, 0) or is_tile(t, 1)):
                    pe.wait_ge(out_ready, t - 2)
                nc.tensor.transpose(ps_out[:, 1 - odd, 0:P], x_norm[:, :], ident[:, :]).then_inc(hT_done, 1)

            def transpose_keys(b):
                if b % 2 == 0:
                    pe.wait_ge(keys_loaded[b // 2], 16)
                if b >= 2:
                    pe.wait_ge(keysT_copied, b - 1)
                for k in range(PER_BLOCK):
                    mm = nc.tensor.transpose(ps_T[:, b % 2, k * P:(k + 1) * P],
                                             keys_in[:, b * PER_BLOCK + k, :], ident[:, :])
                mm.then_inc(keysT_done, 1)

            def score_block(q, odd, b):
                if b == 0:
                    pe.wait_ge(hT_ready, q + 1)
                if is_tile(q, 0) and b % 2 == 0:
                    pe.wait_ge(keysT_hi_ready, b // 2 + 1)
                    pe.wait_ge(keysT_lo_ready, b // 2 + 1)
                if b % 2 == 0 and (not is_tile(q, 0) or b >= SLOTS):
                    pe.wait_ge(leaky_ready, q * PAIRS + (b - SLOTS) // 2 + 1)
                dst = ps_scores[:, b % SLOTS, :]
                nc.tensor.matmul(dst, hT_hi[:, odd, :], keysT_hi[:, cols(b)], start=True, stop=False)
                nc.tensor.matmul(dst, hT_hi[:, odd, :], keysT_lo[:, cols(b)], start=False, stop=False)
                nc.tensor.matmul(dst, hT_lo[:, odd, :], keysT_hi[:, cols(b)], start=False, stop=True) \
                    .then_inc(scores_done, 1)

            def transpose_probs(t, b):
                if b % 2 == 0:
                    pe.wait_ge(probs_ready, t * PAIRS + b // 2 + 1)
                if not is_tile(t, 0) or b >= 2:
                    pe.wait_ge(T_lo_ready, t * BLOCKS + b - 1)
                for k in range(PER_BLOCK):
                    at = (b % 2) * BLOCK + k * P
                    mm = nc.tensor.transpose(ps_T[:, b % 2, k * P:(k + 1) * P],
                                             probs[:, (b // 2) % 2, at:at + P], ident[:, :])
                mm.then_inc(T_done, 1)

            def output_block(t, odd, b):
                pe.wait_ge(T_hi_ready, t * BLOCKS + b + 1)
                pe.wait_ge(T_lo_ready, t * BLOCKS + b + 1)
                if is_tile(t, 0) and b % 2 == 0:
                    pe.wait_ge(keys_lo_ready, b // 2 + 1)
                if b == 0 and not (is_tile(t, 0) or is_tile(t, 1)):
                    pe.wait_ge(out_ready, t - 1)
                o = ps_out[:, odd, :]
                for k in range(PER_BLOCK):
                    c = b * PER_BLOCK + k
                    hi_part = probsT_hi[:, b % T_SLOTS, k * P:(k + 1) * P]
                    lo_part = probsT_lo[:, b % T_SLOTS, k * P:(k + 1) * P]
                    if c < CHUNKS - 1:
                        nc.tensor.matmul(o[:, 0:2 * D], hi_part, keys[:, c, :], start=(c == 0), stop=False)
                        mm = nc.tensor.matmul(o[:, 0:D], lo_part, keys[:, c, 0:D], start=False, stop=False)
                    else:
                        nc.tensor.matmul(o[:, 0:D], lo_part, keys[:, c, 0:D], start=False, stop=False)
                        mm = nc.tensor.matmul(o[:, 0:2 * D], hi_part, keys[:, c, :], start=False, stop=True)
                mm.then_inc(out_done, 1)

            transpose_h(0, 0)
            for b in range(BLOCKS):
                transpose_keys(b)
            pe.wait_ge(scale_steps, PAIRS + 2)
            pe.wait_ge(hT_ready, 1)
            nc.tensor.matmul(ps_out[:, 0, 0:P], ones[:, :], max_diag[:, :], start=True, stop=True) \
                .then_inc(max_spread, 1)

            def step(i, odd, more, this, prev, ahead):
                for j in range(BLOCKS):
                    if more:
                        score_block(i + 1, 1 - odd, j)
                    turned = behind(i, odd, j, T_LAG, this, prev)
                    if turned:
                        transpose_probs(turned[0], turned[2])
                    added = behind(i, odd, j, T_LAG + OUT_LAG, this, prev)
                    if added:
                        output_block(*added)
                    if j == 11 and ahead:
                        transpose_h(i + 2, odd)

            steps(pe, step)

        @block.scalar
        def _(act):
            def copy_keysT(b):
                act.wait_ge(keysT_done, b + 1)
                nc.scalar.activation(keysT[:, cols(b)], ps_T[:, b % 2, :], ACT.Copy).then_inc(keysT_copied, 1)

            def split_keysT_hi(p):
                act.wait_ge(keysT_copied, 2 * p + 2)
                nc.scalar.activation(keysT_hi[:, pair_cols(p)], keysT[:, pair_cols(p)], ACT.Copy,
                                     scale=key_scale[:, :]).then_inc(keysT_hi_ready, 1)

            def split_keys_hi(p):
                c = slice(p * PER_PAIR, (p + 1) * PER_PAIR)
                nc.scalar.activation(keys[:, c, 0:D], keys_in[:, c, :], ACT.Copy, scale=key_scale[:, :]) \
                    .then_inc(keys_hi_ready, 1)

            def relu(q, odd, b):
                act.wait_ge(scores_done, q * BLOCKS + b + 1)
                if not (is_tile(q, 0) or is_tile(q, 1)):
                    act.wait_ge(probs_ready, (q - 2) * PAIRS + b // 2 + 1)
                if is_tile(q, 1):
                    act.wait_ge(keysT_lo_ready, b // 2 + 1)
                nc.scalar.activation(scores[:, odd, cols(b)], ps_scores[:, b % SLOTS, :], ACT.Relu,
                                     scale=1.0 / SLOPE - 1.0).then_inc(relu_ready, 1)

            def exponentials(t, odd, p):
                if p == 0:
                    act.wait_ge(neg_max_ready, t + 1)
                    if not (is_tile(t, 0) or is_tile(t, 1)):
                        act.wait_ge(sum_ready, t - 1)
                if not is_tile(t, 0) or p >= 2:
                    act.wait_ge(T_done, t * BLOCKS + 2 * p - 2)
                nc.scalar.activation(probs[:, p % 2, :], scores[:, odd, p * PAIR:(p + 1) * PAIR], ACT.Exp,
                                     bias=neg_max[:, odd:odd + 1], scale=1.0,
                                     accum_out=pair_sum[:, odd, p:p + 1]) \
                    .then_inc(probs_ready, 1)

            def split_probs_hi(t, b):
                act.wait_ge(T_done, t * BLOCKS + b + 1)
                if not is_tile(t, 0) or b >= T_SLOTS:
                    act.wait_ge(out_done, t * BLOCKS + b - T_SLOTS + 1)
                nc.scalar.activation(probsT_hi[:, b % T_SLOTS, :], ps_T[:, b % 2, :], ACT.Copy,
                                     scale=2.0 ** PROB_BITS).then_inc(T_hi_ready, 1)

            for b in range(BLOCKS):
                copy_keysT(b)
            act.wait_ge(scale_steps, SCALED)
            split_keysT_hi(0)
            split_keysT_hi(1)

            def step(i, odd, more, this, prev, ahead):
                for j in range(BLOCKS):
                    if is_tile(i, -1) and j % 2 == 0 and j // 2 + 2 < PAIRS:
                        split_keysT_hi(j // 2 + 2)
                    if more:
                        relu(i + 1, 1 - odd, j)
                    if is_tile(i, -1) and j % 2 == 1:
                        split_keys_hi(j // 2)
                    turned = behind(i, odd, j, T_LAG, this, prev)
                    if turned:
                        split_probs_hi(turned[0], turned[2])
                    if j % 2 == 0:
                        made = behind(i, odd, j, T_LAG - 2, this, prev)
                        if made:
                            exponentials(made[0], made[1], made[2] // 2)

            steps(act, step)

        @block.vector
        def _(dve):
            def statistics(t):
                dve.wait_ge(x_loaded, 16 * t + 16)
                nc.vector.bn_stats(bn[:, :], x_in[:, :]).then_inc(bn_done, 1)
                dve.wait_ge(bn_done, t + 1)
                if not is_tile(t, 0):
                    dve.wait_ge(rstd_ready, t)
                dve.nop(nofuse=True)
                nc.vector.bn_aggr(mean_var[:, :], bn[:, :]).then_inc(stats_ready, 1)

            def normalise(t):
                dve.wait_ge(rstd_ready, t + 1)
                if not is_tile(t, 0):
                    dve.wait_ge(hT_done, t)
                nc.vector.tensor_scalar(x_norm[:, :], x_in[:, :], mean_var[:, 0:1], rstd[:, 0:1],
                                        ALU.subtract, ALU.mult).then_inc(norm_ready, 1)

            def split_h(t, odd):
                dve.wait_ge(hT_done, t + 1)
                if not (is_tile(t, 0) or is_tile(t, 1)):
                    dve.wait_ge(scores_done, (t - 1) * BLOCKS)
                src = ps_out[:, 1 - odd, 0:P]
                nc.vector.tensor_scalar(hT_hi[:, odd, :], src, 0.0, None, ALU.max).then_inc(hT_hi_ready, 1)
                dve.wait_ge(hT_hi_ready, t + 1)
                nc.vector.scalar_tensor_tensor(out=hT_lo[:, odd, :], in0=src, scalar=0.0, in1=hT_hi[:, odd, :],
                                               op0=ALU.max, op1=ALU.subtract).then_inc(hT_ready, 1)

            def find_scales():
                for p in range(PAIRS):
                    dve.wait_ge(keys_loaded[p], 16)
                    nc.vector.tensor_reduce(load_max[:, p:p + 1], keys_in[:, p * PER_PAIR:(p + 1) * PER_PAIR, :],
                                            axis=AX.XY, op=ALU.max, apply_absolute_value=True) \
                        .then_inc(scale_steps, 1)
                dve.wait_ge(scale_steps, PAIRS)
                nc.vector.tensor_reduce(part_max[:, :], load_max[:, :], axis=AX.X, op=ALU.max) \
                    .then_inc(scale_steps, 1)
                dve.wait_ge(scale_steps, PAIRS + 1)
                nc.vector.tensor_scalar(max_diag[:, :], ident[:, :], part_max[:, 0:1], None, ALU.mult) \
                    .then_inc(scale_steps, 1)
                dve.wait_ge(max_spread, 1)
                nc.vector.tensor_reduce(key_max[:, :], ps_out[:, 0, 0:P], axis=AX.X, op=ALU.max) \
                    .then_inc(scale_steps, 1)
                dve.wait_ge(scale_steps, PAIRS + 3)
                nc.vector.tensor_scalar(key_pow2[:, :].bitcast(int32), key_max[:, :].bitcast(int32), EXPONENT, None,
                                        ALU.bitwise_and).then_inc(scale_steps, 1)
                dve.wait_ge(scale_steps, PAIRS + 4)
                nc.vector.tensor_scalar(key_pow2[:, :], key_pow2[:, :], TINY, None, ALU.max) \
                    .then_inc(scale_steps, 1)
                dve.wait_ge(scale_steps, PAIRS + 5)
                nc.vector.reciprocal(inv_pow2[:, :], key_pow2[:, :]).then_inc(scale_steps, 1)
                nc.vector.tensor_scalar(score_scale[:, :], key_pow2[:, :], SLOPE * 2.0 ** (-H_BITS - KEY_BITS), None,
                                        ALU.mult).then_inc(scale_steps, 1)
                nc.vector.tensor_scalar(out_scale[:, :], key_pow2[:, :], 2.0 ** (-PROB_BITS - KEY_BITS), None,
                                        ALU.mult).then_inc(scale_steps, 1)
                dve.wait_ge(scale_steps, PAIRS + 6)
                nc.vector.tensor_scalar(key_scale[:, :], inv_pow2[:, :], 2.0 ** KEY_BITS, None, ALU.mult) \
                    .then_inc(scale_steps, 1)
                dve.wait_ge(scale_steps, SCALED)

            def split_keysT_lo(p):
                dve.wait_ge(keysT_hi_ready, p + 1)
                c = pair_cols(p)
                nc.vector.scalar_tensor_tensor(out=keysT_lo[:, c], in0=keysT[:, c], scalar=key_scale[:, 0:1],
                                               in1=keysT_hi[:, c], op0=ALU.mult, op1=ALU.subtract) \
                    .then_inc(keysT_lo_ready, 1)

            def split_keys_lo(p):
                c = slice(p * PER_PAIR, (p + 1) * PER_PAIR)
                dve.wait_ge(keys_hi_ready, p + 1)
                nc.vector.scalar_tensor_tensor(out=keys[:, c, D:2 * D], in0=keys_in[:, c, :], scalar=key_scale[:, 0:1],
                                               in1=keys[:, c, 0:D], op0=ALU.mult, op1=ALU.subtract) \
                    .then_inc(keys_lo_ready, 1)

            def make_mask(q, p):
                k = p // 2
                dve.wait_ge(adj_loaded[k % 2], (q * (LOADS // 2) + k // 2 + 1) * 16)
                if not is_tile(q, 0) or p >= 2:
                    dve.wait_ge(masked_ready, q * BLOCKS + 2 * p - 2)
                nc.vector.tensor_scalar(mask[:, p % 2, :], adj_in[:, k % 2, (p % 2) * PAIR:(p % 2 + 1) * PAIR],
                                        0.0, MASKED, ALU.is_le, ALU.mult).then_inc(mask_ready, 1)

            def leaky(q, odd, p):
                dve.wait_ge(masked_ready, q * BLOCKS + 2 * p + 2)
                if p == 0 and not is_tile(q, 0):
                    dve.wait_ge(max_ready, q)
                dve.nop(nofuse=True)
                s = scores[:, odd, p * PAIR:(p + 1) * PAIR]
                slots = bass.ds(2 * p % SLOTS, 2)
                nc.vector.tensor_tensor_reduce(out=s, in0=ps_scores[:, slots, :].rearrange("p s k -> p (s k)"), in1=s,
                                               scale=score_scale[:, 0:1], scalar=LOWEST, op0=ALU.add, op1=ALU.max,
                                               accum_out=pair_max[:, p:p + 1]).then_inc(leaky_ready, 1)

            def split_probs_lo(t, b):
                dve.wait_ge(T_hi_ready, t * BLOCKS + b + 1)
                nc.vector.scalar_tensor_tensor(out=probsT_lo[:, b % T_SLOTS, :], in0=ps_T[:, b % 2, :],
                                               scalar=2.0 ** PROB_BITS, in1=probsT_hi[:, b % T_SLOTS, :],
                                               op0=ALU.mult, op1=ALU.subtract).then_inc(T_lo_ready, 1)

            def maximum(q, odd):
                dve.wait_ge(leaky_ready, (q + 1) * PAIRS)
                nc.vector.tensor_reduce(row_max[:, :], pair_max[:, :], axis=AX.X, op=ALU.max).then_inc(max_ready, 1)
                dve.wait_ge(max_ready, q + 1)
                if not (is_tile(q, 0) or is_tile(q, 1)):
                    dve.wait_ge(probs_ready, (q - 1) * PAIRS)
                nc.vector.tensor_scalar(neg_max[:, odd:odd + 1], row_max[:, :], -1.0, None, ALU.mult) \
                    .then_inc(neg_max_ready, 1)

            def weigh(t, odd):
                dve.wait_ge(probs_ready, (t + 1) * PAIRS)
                nc.vector.tensor_reduce(row_sum[:, :], pair_sum[:, odd, :], axis=AX.X, op=ALU.add).then_inc(sum_ready, 1)
                dve.wait_ge(sum_ready, t + 1)
                nc.vector.reciprocal(inv_sum[:, :], row_sum[:, :]).then_inc(inv_ready, 1)
                dve.wait_ge(inv_ready, t + 1)
                nc.vector.tensor_scalar(weight[:, :], inv_sum[:, :], out_scale[:, 0:1], None, ALU.mult) \
                    .then_inc(weight_ready, 1)

            def finish(t, odd):
                dve.wait_ge(out_done, (t + 1) * BLOCKS)
                dve.wait_ge(res_loaded, 16 * t + 16)
                dve.wait_ge(weight_ready, t + 1)
                nc.vector.scalar_tensor_tensor(out=out_lo[:, :], in0=ps_out[:, odd, D:2 * D], scalar=weight[:, 0:1],
                                               in1=x_res[:, :], op0=ALU.mult, op1=ALU.add).then_inc(lo_scaled, 1)
                dve.wait_ge(lo_scaled, t + 1)
                if not is_tile(t, 0):
                    dve.wait_ge(stored, 16 * t)
                nc.vector.scalar_tensor_tensor(out=out_tile[:, :], in0=ps_out[:, odd, 0:D], scalar=weight[:, 0:1],
                                               in1=out_lo[:, :], op0=ALU.mult, op1=ALU.add).then_inc(out_ready, 1)

            dve.wait_ge(consts_ready, CONSTS)
            statistics(0)
            normalise(0)
            split_h(0, 0)
            find_scales()
            split_keysT_lo(0)
            make_mask(0, 0)

            def step(i, odd, more, this, prev, ahead):
                for j in range(BLOCKS):
                    p = j // 2
                    if is_tile(i, -1) and j % 2 == 0 and p + 1 < PAIRS:
                        split_keysT_lo(p + 1)
                    if is_tile(i, 0) and j % 2 == 0:
                        split_keys_lo(p)
                    turned = behind(i, odd, j, T_LAG, this, prev)
                    if turned:
                        split_probs_lo(turned[0], turned[2])
                    if more and j % 2 == 0:
                        if p + 1 < PAIRS:
                            make_mask(i + 1, p + 1)
                        elif not is_tile(i, TILES - 2):
                            make_mask(i + 2, 0)
                    if ahead:
                        if j == 4:
                            statistics(i + 2)
                        if j == 9:
                            normalise(i + 2)
                        if j == 13:
                            split_h(i + 2, odd)
                    if prev and j == 2:
                        weigh(i - 1, 1 - odd)
                    if prev and j == 6:
                        finish(i - 1, 1 - odd)
                    if more and j % 2 == 1:
                        leaky(i + 1, 1 - odd, p)
                if more:
                    maximum(i + 1, 1 - odd)

            steps(dve, step)


_INS = ["x", "adj", "L0_gnn_ks"]


def kernel(**inputs):
    import numpy as _np
    import concourse.bacc as _bacc
    from concourse import mybir as _mybir
    from concourse.bass_utils import run_bass_kernel_spmd as _run

    nc = _bacc.Bacc("TRN2", target_bir_lowering=False, num_devices=1)
    arrays, args = {}, []
    for name in _INS:
        a = _np.ascontiguousarray(inputs[name])
        arrays[f"in_{name}_dram"] = a
        args.append(nc.dram_tensor(f"in_{name}_dram", a.shape, _mybir.dt.from_np(a.dtype), kind="ExternalInput").ap())
    shape = inputs["x"].shape
    args.append(nc.dram_tensor("out_dram", shape, _mybir.dt.float32, kind="ExternalOutput").ap())
    gat_kernel(nc, *args)
    r = _run(nc, [arrays], core_ids=[0])
    return r.results[0]["out_dram"]
```
